# Optimizing a Trainium2 kernel written in Bass

```python
import numpy as np
import jax
import jax.numpy as jnp

def _softmax(x, axis=-1):
    return jax.nn.softmax(x, axis=axis)

def _gelu(x):
    return jax.nn.gelu(x, approximate=True)

def _silu(x):
    return jax.nn.silu(x)

def _sigmoid(x):
    return jax.nn.sigmoid(x)

def _layernorm(x, axis=-1, eps=1e-05):
    m = jnp.mean(x, axis=axis, keepdims=True)
    v = jnp.var(x, axis=axis, keepdims=True)
    return (x - m) / jnp.sqrt(v + eps)

def _scatter_add(tgt, idx, src, axis=0):
    return tgt.at[idx].add(src)

def _segment_sum(src, seg, n):
    return jax.ops.segment_sum(src, seg, n)
kernel_name = 'mk_gps_d1_gnn_r16_e137e6'

def setup_inputs(seed: int=0):
    np.random.seed(seed)
    _w = jnp.asarray

    def _rec_inputs():
        import jax
        import jax.numpy as jnp
        _gk = jax.random.key(seed)
        x = -6.415e-05 + 1 * jax.random.normal(jax.random.fold_in(_gk, 1), (625, 512), jnp.float32)
        _s = jax.random.randint(jax.random.fold_in(_gk, 2), (5000,), 0, 625, jnp.int32)
        _d = jax.random.randint(jax.random.fold_in(_gk, 3), (5000,), 0, 625, jnp.int32)
        _loop = jnp.arange(625, dtype=jnp.int32)
        src = jnp.concatenate([_s, _d, _loop])
        dst = jnp.concatenate([_d, _s, _loop])
        _o = jnp.argsort(dst, stable=True)
        src = src[_o]
        dst = dst[_o]
        edge_attr_512 = -8.16379e-05 + 0.999858 * jax.random.normal(jax.random.fold_in(_gk, 12), (10625, 512), jnp.float32)
        return (x, src, dst, edge_attr_512)
    x, src, dst, edge_attr_512 = _rec_inputs()

    def _L0_gnn_setup():
        import jax, jax.numpy as jnp
        import numpy as np
        N_NODES = 1250
        N_EDGES = 12500
        N_SEG = 16
        EXTENT = 32
        N_PATHS = 64
        OP_SIZE = N_SEG * EXTENT
        key = jax.random.key(seed)
        k1, k2, k3, k4, k5, k6 = jax.random.split(key, 6)
        x_nodes = jax.random.normal(k1, (N_NODES, OP_SIZE), dtype=jnp.float32)
        x_edges = jax.random.normal(k2, (N_EDGES, OP_SIZE), dtype=jnp.float32)
        path_coeffs = jax.random.normal(k3, (N_PATHS,), dtype=jnp.float32)
        src = jax.random.randint(k4, (N_EDGES,), 0, N_NODES, dtype=jnp.int64)
        dst = jax.random.randint(k5, (N_EDGES,), 0, N_NODES, dtype=jnp.int64)
        path_indices = jax.random.randint(k6, (N_PATHS, 3), 0, N_SEG, dtype=jnp.int64)
        return {'x_nodes': x_nodes, 'x_edges': x_edges, 'path_coeffs': path_coeffs, 'src': src, 'dst': dst, 'path_indices': path_indices}
    _L0_gnn_all = _L0_gnn_setup()
    _L0_gnn_in = {k: v for k, v in _L0_gnn_all.items() if k in ('path_coeffs', 'path_indices')}
    del _L0_gnn_all

    def _L0_mix_setup():
        import jax, jax.numpy as jnp
        import numpy as np
        B, S, H = (4, 512, 512)
        NH, HD = (8, 64)
        FD = HD // 2
        key = jax.random.key(seed)
        k1, k2, k3, k4 = jax.random.split(key, 4)
        x = jax.random.normal(k1, (B, S, H), dtype=jnp.float32)
        W_qkv = jax.random.normal(k2, (H, 3 * H), dtype=jnp.float32) * (1.0 / np.sqrt(H))
        random_matrix = jax.random.normal(k3, (HD, FD), dtype=jnp.float32) * (1.0 / np.sqrt(HD))
        W_out = jax.random.normal(k4, (H, H), dtype=jnp.float32) * (1.0 / np.sqrt(H))
        b_out = jnp.zeros((H,), dtype=jnp.float32)
        return {'x': x, 'W_qkv': W_qkv, 'random_matrix': random_matrix, 'W_out': W_out, 'b_out': b_out}
    _L0_mix_all = _L0_mix_setup()
    _L0_mix_in = {k: v for k, v in _L0_mix_all.items() if k in ('W_qkv', 'random_matrix', 'W_out', 'b_out')}
    del _L0_mix_all

    def _L0_ffn_setup():
        import jax, jax.numpy as jnp
        import numpy as np
        E = 64
        K = 6
        NS = 2
        D = 512
        F = 512

        def _swiglu_ffn(x, wg, wu, wd):
            return jax.nn.silu(x @ wg) * (x @ wu) @ wd
        key = jax.random.key(seed)
        ks = jax.random.split(key, 8)
        s = 0.02
        return {'hidden_states': jax.random.normal(ks[0], (2, 1024, D), dtype=jnp.float32), 'Wr': jax.random.normal(ks[1], (D, E), dtype=jnp.float32) * s, 'sWg': jax.random.normal(ks[2], (NS, D, F), dtype=jnp.float32) * s, 'sWu': jax.random.normal(ks[3], (NS, D, F), dtype=jnp.float32) * s, 'sWd': jax.random.normal(ks[4], (NS, F, D), dtype=jnp.float32) * s, 'Wg': jax.random.normal(ks[5], (E, D, F), dtype=jnp.float32) * s, 'Wu': jax.random.normal(ks[6], (E, D, F), dtype=jnp.float32) * s, 'Wd': jax.random.normal(ks[7], (E, F, D), dtype=jnp.float32) * s}
    _L0_ffn_all = _L0_ffn_setup()
    _L0_ffn_in = {k: v for k, v in _L0_ffn_all.items() if k in ('Wr', 'sWg', 'sWu', 'sWd', 'Wg', 'Wu', 'Wd')}
    del _L0_ffn_all
    return {'x': x, 'src': src, 'dst': dst, 'edge_attr_512': edge_attr_512, 'L0_gnn_path_coeffs': _L0_gnn_in['path_coeffs'], 'L0_gnn_path_indices': _L0_gnn_in['path_indices'], 'L0_mix_W_qkv': _L0_mix_in['W_qkv'], 'L0_mix_random_matrix': _L0_mix_in['random_matrix'], 'L0_mix_W_out': _L0_mix_in['W_out'], 'L0_mix_b_out': _L0_mix_in['b_out'], 'L0_ffn_Wr': _L0_ffn_in['Wr'], 'L0_ffn_sWg': _L0_ffn_in['sWg'], 'L0_ffn_sWu': _L0_ffn_in['sWu'], 'L0_ffn_sWd': _L0_ffn_in['sWd'], 'L0_ffn_Wg': _L0_ffn_in['Wg'], 'L0_ffn_Wu': _L0_ffn_in['Wu'], 'L0_ffn_Wd': _L0_ffn_in['Wd']}

def reference(x, src, dst, edge_attr_512, L0_gnn_path_coeffs, L0_gnn_path_indices, L0_mix_W_qkv, L0_mix_random_matrix, L0_mix_W_out, L0_mix_b_out, L0_ffn_Wr, L0_ffn_sWg, L0_ffn_sWu, L0_ffn_sWd, L0_ffn_Wg, L0_ffn_Wu, L0_ffn_Wd):
    import jax
    import jax.numpy as jnp

    def _L0_gnn_ref(x_nodes, x_edges, path_coeffs, src, dst, path_indices):
        import jax, jax.numpy as jnp
        import numpy as np
        N_NODES = 1250
        N_EDGES = 12500
        N_SEG = 16
        EXTENT = 32
        N_PATHS = 64
        OP_SIZE = N_SEG * EXTENT
        n_nodes = x_nodes.shape[0]
        x1 = x_nodes[src].reshape(-1, N_SEG, EXTENT)
        x2 = x_edges.reshape(-1, N_SEG, EXTENT)
        i1, i2, i3 = (path_indices[:, 0], path_indices[:, 1], path_indices[:, 2])
        contrib = path_coeffs[None, :, None] * x1[:, i1, :] * x2[:, i2, :]
        edge_out = jnp.zeros((x2.shape[0], N_SEG, EXTENT), x_nodes.dtype).at[:, i3, :].add(contrib)
        out = jnp.zeros((n_nodes, OP_SIZE), x_nodes.dtype).at[dst].add(edge_out.reshape(-1, OP_SIZE))
        return out

    def _L0_mix_ref(x, W_qkv, random_matrix, W_out, b_out):
        import jax, jax.numpy as jnp
        import numpy as np
        B, S, H = (4, 512, 512)
        NH, HD = (8, 64)
        FD = HD // 2
        b, s, h = x.shape
        qkv = (x @ W_qkv).reshape(b, s, 3, NH, HD)
        q, k, v = (qkv[:, :, 0], qkv[:, :, 1], qkv[:, :, 2])
        q_prime = jax.nn.elu(q @ random_matrix) + 1.0
        k_prime = jax.nn.elu(k @ random_matrix) + 1.0
        kv = jnp.einsum('bshd,bshf->bhdf', k_prime, v)
        z = jnp.einsum('bshd,bhdf->bshf', q_prime, kv)
        normalizer = jnp.einsum('bshd,bhd->bsh', q_prime, k_prime.sum(axis=1))
        z = z / (normalizer[..., None] + 1e-06)
        z = z.reshape(b, s, h)
        return z @ W_out + b_out

    def _L0_ffn_ref(hidden_states, Wr, sWg, sWu, sWd, Wg, Wu, Wd):
        import jax, jax.numpy as jnp
        import numpy as np
        E = 64
        K = 6
        NS = 2
        D = 512
        F = 512

        def _swiglu_ffn(x, wg, wu, wd):
            return jax.nn.silu(x @ wg) * (x @ wu) @ wd
        B, S, d = hidden_states.shape
        x = hidden_states.reshape(-1, d)
        N = x.shape[0]
        shared = jnp.zeros_like(x)
        for e in range(NS):
            shared = shared + _swiglu_ffn(x, sWg[e], sWu[e], sWd[e])
        logits = x @ Wr
        probs = jax.nn.softmax(logits, axis=-1)
        top_w, top_i = jax.lax.top_k(probs, K)
        top_w = top_w / jnp.sum(top_w, axis=-1, keepdims=True)
        gate = jnp.zeros((N, E), dtype=x.dtype).at[jnp.arange(N)[:, None], top_i].set(top_w)
        routed = jnp.zeros_like(x)
        for e in range(E):
            routed = routed + _swiglu_ffn(x, Wg[e], Wu[e], Wd[e]) * gate[:, e:e + 1]
        out = (shared + routed + x).reshape(B, S, d)
        return out
    xn = _layernorm(x, axis=-1)
    x = x + _L0_gnn_ref(xn, edge_attr_512, L0_gnn_path_coeffs, src, dst, L0_gnn_path_indices) + _L0_mix_ref(xn[None], L0_mix_W_qkv, L0_mix_random_matrix, L0_mix_W_out, L0_mix_b_out)[0]
    x = x + _L0_ffn_ref(_layernorm(x, axis=-1)[None], L0_ffn_Wr, L0_ffn_sWg, L0_ffn_sWu, L0_ffn_sWd, L0_ffn_Wg, L0_ffn_Wu, L0_ffn_Wd)[0]
    return x

_drawn_inputs = setup_inputs


def setup_inputs(seed=0):
    import zlib

    import numpy as np

    out = dict(_drawn_inputs(seed))
    spreads = {'L0_mix_b_out': (0.0, 0.611)}
    factors = {'L0_mix_W_qkv': 8.0,
     'L0_mix_random_matrix': 8.0,
     'L0_mix_W_out': 8.0,
     'L0_ffn_Wr': 8.0,
     'L0_ffn_sWg': 7.164,
     'L0_ffn_sWu': 7.005,
     'L0_ffn_sWd': 7.006,
     'L0_ffn_Wg': 8.0,
     'L0_ffn_Wu': 8.0,
     'L0_ffn_Wd': 8.0}
    for name, (base, spread) in spreads.items():
        noise = np.random.default_rng([zlib.crc32(name.encode()), seed]).standard_normal(out[name].shape)
        drawn = base * np.exp(spread * noise) if base else spread * noise
        out[name] = jnp.asarray(drawn.astype(out[name].dtype))
    for name, factor in factors.items():
        out[name] = (out[name] * factor).astype(out[name].dtype)
    return out
```

```python
from contextlib import ExitStack

import concourse.bass as bass
from concourse import mybir

F32 = mybir.dt.float32
BF16 = mybir.dt.bfloat16
I32 = mybir.dt.int32
ALU = mybir.AluOpType
ACT = mybir.ActivationFunctionType
AX = mybir.AxisListType.X

N = 625
D = 512
E = 10625
SEG, EXT, PATHS = 16, 32, 64
NH, HD, FD = 8, 64, 32
NX, TOPK, NS = 64, 6, 2
EPS = 1e-5

TT, TR, DC = 5, 125, 4
HALVES = ((0, 313), (313, 312))

ET = -(-E // 128)
LAST_ROW = E - 128
W = 64
NW = -(-N // W)
PAIRS = NW * ET
GROUP = 8
JC = 7
BLOCKS, DUOS = 8, 7
FIELDS = 6
PH = PATHS // 2

CAP = 64
HF = D // 2
MAX_TILES = NX + (N * TOPK - NX) // CAP
T_BLOCKS, T_DUOS = 8, 8
assert T_BLOCKS * T_DUOS * 2 >= MAX_TILES
PLACES = 8
RING = 4
SLOT = 3 * DC * D
ROWS = N + CAP
NCHUNK = 4
MOVES = [(i, w) for i in range(TT) for w in range(i * TR // W, (i * TR + TR - 1) // W + 1)]


def layout(ctx, nc):
    m = {}

    def sb(name, shape, dt=F32):
        m[name] = ctx.enter_context(nc.sbuf_tensor(name, shape, dt))
        return m[name]

    arena = sb("arena", [128, 32768])
    m["prod"] = arena[:, 0:16384].rearrange("p (h g c) -> p h g c", h=2, g=GROUP)
    m["x1"] = arena[:, 16384:24576].rearrange("p (b g d) -> p b g d", b=2, g=GROUP)
    m["x2"] = arena[:, 24576:32768].rearrange("p (b g d) -> p b g d", b=2, g=GROUP)
    m["wqkv"] = arena[:, 0:6144].rearrange("p (c n) -> p c n", c=DC)
    m["wout"] = arena[:, 6144:8192].rearrange("p (c n) -> p c n", c=DC)
    m["qkT"] = arena[:, 8192:13192].rearrange("p (c n) -> p c n", c=8)
    m["v"] = arena[0:TR, 13192:15792].rearrange("p (t h c) -> p t h c", t=TT, h=NH)
    m["node"] = arena[:, 24576:29696].rearrange("p (w d) -> p w d", w=NW)
    m["move"] = arena[:, 29696:29696 + len(MOVES) * TR].rearrange("p (i r) -> p i r", r=TR)
    ring = arena[:, 0:RING * SLOT].rearrange("p (s w c n) -> p s w c n", s=RING, w=3, c=DC)
    m["ring"] = ring

    low = sb("low", [128, 10240])
    m["xn"] = low[0:TR, 0:2560].rearrange("p (t d) -> p t d", t=TT)
    m["z"] = low[0:TR, 2560:5120].rearrange("p (t d) -> p t d", t=TT)
    m["zT"] = low[:, 5120:7620].rearrange("p (c n) -> p c n", c=DC)
    m["qp"] = low[:, 7620:8870].rearrange("p (g n) -> p g n", g=2)
    m["kp"] = low[0:TR, 8870:10150].rearrange("p (t c) -> p t c", t=TT)
    m["sums"] = low[:, :].rearrange("p (w h n) -> p w h n", w=NW, h=2)
    m["hS"] = low[:, 2560:5060].rearrange("p (c n) -> p c n", c=DC)
    for i, name in enumerate(("xg", "xgT", "sg", "h", "hT", "y")):
        a = 5120 + 512 * i
        m[name] = low[:, a:a + 512].rearrange("p (b n) -> p b n", b=2)
    m["sgS"] = low[:, 8192:8192 + 626].rearrange("p (b n) -> p b n", b=2)
    m["rtab"] = low[0:TR, 8832:8832 + 960].bitcast(BF16).rearrange("p (e t c) -> p e t c", e=NX, t=TT)

    sb("x", [TR, TT, D])
    m["xT"] = sb("xT_", [128, DC * N])[:, :].rearrange("p (c n) -> p c n", c=DC)
    return m


def gps_layer(nc, x, src, dst, edge, coeffs, paths, wqkv, rm, wout, bout,
              wr, swg, swu, swd, wg, wu, wd, out):
    with ExitStack() as ctx:
        m = layout(ctx, nc)

        def sb(name, shape, dt=F32):
            return ctx.enter_context(nc.sbuf_tensor(name, shape, dt))

        def sem(name):
            return ctx.enter_context(nc.semaphore(name))

        bank = [ctx.enter_context(nc.psum_tensor(f"bank{i}", [128, 512], F32)) for i in range(8)]

        xn_d = nc.dram_tensor("xn_d", (N, D), F32).ap()
        xr_d = nc.dram_tensor("xr_d", (ROWS, D), F32).ap()
        acc_d = nc.dram_tensor("acc_d", (ROWS, D), F32).ap()
        xr_half = xr_d.rearrange("n (h d) -> (n h) d", h=2)
        acc_half = acc_d.rearrange("n (h d) -> (n h) d", h=2)
        ends_d = nc.dram_tensor("ends_d", (1, NX), I32).ap()
        items_d = nc.dram_tensor("items_d", (FIELDS * JC, 128), I32).ap()
        tiles_d = nc.dram_tensor("tiles_d", (128, 4), I32).ap()
        items_row = items_d.rearrange("(o f) p -> o (f p)", o=1)

        x_sb, xT, xn = m["x"], m["xT"], m["xn"]
        prod, x1, x2, sums, node, move = m["prod"], m["x1"], m["x2"], m["sums"], m["node"], m["move"]
        wqkv_sb, wout_sb, qkT, v, z, zT, qp, kp = (m[k] for k in ("wqkv", "wout", "qkT", "v", "z", "zT", "qp", "kp"))
        ring, hS = m["ring"], m["hS"]

        iota = sb("iota", [128, 768])
        prow = sb("prow", [128, 1])
        jcol = sb("jcol", [128, JC])
        ident = sb("ident", [128, 128])
        tri = sb("tri", [128, 128], BF16)
        ones = sb("ones", [128, 128], BF16)
        w64 = sb("w64", [128, NW + 2])
        quad = sb("quad", [128, 5])
        qmask = sb("qmask", [128, 4])
        zero_l = sb("zero_l", [1, 128], BF16)
        zero_r = sb("zero_r", [1, 512], BF16)
        eps_c = sb("eps_c", [128, 1])
        place = sb("place", [128, 2])
        tri_f = sb("tri_f", [128, 128])

        stats = sb("stats", [128, TT, 6])
        mv = sb("mv", [128, TT, 2])
        rstd = sb("rstd", [128, TT])
        pair = ctx.enter_context(nc.sbuf_tensor("pair", [128, 2, 8, W], F32))
        srcT = sb("srcT", [128, ET], I32)
        dstT = sb("dstT", [128, ET])
        ssel = sb("ssel", [128, 2 * GROUP], I32)
        dsel = sb("dsel", [128, 2, GROUP])
        poff = sb("poff", [1, PATHS * 2], I32)
        toff = sb("toff", [1, PATHS], I32)
        coef = sb("coef", [128, PATHS])
        pm = sb("pm", [128, 1])
        small = sb("small", [128, 64])

        pad = m["arena"][:, 15792:16384]
        early = m["arena"][:, 16384:32768]
        edge_i = early[0:ET, 0:256].bitcast(I32).rearrange("p (a n) -> p a n", a=2)
        edge_f = early[0:ET, 256:512].rearrange("p (a n) -> p a n", a=2)
        pidx_i = early[:, 512:704].bitcast(I32)

        ge = early[:, 1088:1088 + 462].bitcast(BF16).rearrange("p (w t) -> p w t", w=NW + 1)
        cnt = early[:, 1600:1600 + 924].rearrange("p (w t) -> p w t", w=NW + 1)
        active = early[:, 2560:3400]
        upto = early[:, 3400:4240]
        junk = early[:, 4240:5080]
        qj = early[:, 5080:5087]
        wcmp = early[:, 5100:5310].rearrange("p (a c w) -> p a c w", a=3, c=JC)
        wj = early[:, 5320:5341].rearrange("p (a c) -> p a c", a=3)
        j3 = early[:, 5350:5371].rearrange("p (a c) -> p a c", a=3)
        fld = early[:, 5376:5376 + FIELDS * JC].rearrange("p (f c) -> p f c", f=FIELDS)
        itemT = early[0:FIELDS * JC, 5440:5568].bitcast(I32)
        rm2 = early[:, 5568:5632]
        bout_b = early[0:TR, 5632:6144]
        elu_q = early[:, 6144:6144 + 1250].rearrange("p (a n) -> p a n", a=2)
        elu_k = early[0:TR, 7424:7936].rearrange("p (a n) -> p a n", a=2)
        kvm = early[:, 7936:8456].rearrange("p (g h c) -> p g h c", g=2, h=4)
        recip = early[0:TR, 8460:8500].rearrange("p (t h) -> p t h", t=TT)
        recip2 = early[0:TR, 8500:8540].rearrange("p (t h) -> p t h", t=TT)
        zeros_b = early[:, 8576:9088]

        s_iota = sem("s_iota")
        s_const = sem("s_const")
        s_x = sem("s_x")
        s_edge = sem("s_edge")
        s_path = sem("s_path")
        s_wqkv = sem("s_wqkv")
        s_wout = sem("s_wout")
        s_rm = sem("s_rm")
        s_rmz = sem("s_rmz")
        s_bout = sem("s_bout")
        s_dummy = sem("s_dummy")
        s_edgef = sem("s_edgef")
        s_edgeT = sem("s_edgeT")
        s_edgeS = sem("s_edgeS")
        s_ge = sem("s_ge")
        s_cnt = sem("s_cnt")
        s_cnts = sem("s_cnts")
        s_fld = sem("s_fld")
        s_fldT = sem("s_fldT")
        s_fldi = sem("s_fldi")
        s_items = sem("s_items")
        s_var = sem("s_var")
        s_std = sem("s_std")
        s_xn = sem("s_xn")
        s_xnd = sem("s_xnd")
        s_dve = sem("s_dve")
        s_poff = sem("s_poff")
        s_xTp = sem("s_xTp")
        s_xT = sem("s_xT")
        s_qkp = sem("s_qkp")
        s_qk = sem("s_qk")
        s_vp = sem("s_vp")
        s_v = sem("s_v")
        s_qfp = sem("s_qfp")
        s_qmin = sem("s_qmin")
        s_qexp = sem("s_qexp")
        s_q = sem("s_q")
        s_kfp = sem("s_kfp")
        s_kmin = sem("s_kmin")
        s_kexp = sem("s_kexp")
        s_k = sem("s_k")
        s_kvp = sem("s_kvp")
        s_kv = sem("s_kv")
        s_zp = sem("s_zp")
        s_z = sem("s_z")
        s_zTp = sem("s_zTp")
        s_zT = sem("s_zT")
        s_mixp = sem("s_mixp")
        s_mix = sem("s_mix")

        s_x2 = [sem(f"s_x2_{b}") for b in range(2)]
        s_x1 = [sem(f"s_x1_{b}") for b in range(2)]
        s_sel = sem("s_sel")
        s_prod = sem("s_prod")
        s_item = [sem(f"s_item{h}") for h in range(2)]
        s_flush = [sem(f"s_flush{h}") for h in range(2)]
        s_zsum = sem("s_zsum")
        s_flushed = sem("s_flushed")
        s_R = sem("s_node")
        s_move = sem("s_move")
        s_pm = sem("s_pm")
        s_comb = sem("s_comb")
        s_gnn = sem("s_gnn")
        passed = {k: sem(f"passed_{k}") for k in ("pe", "act", "dve", "pool", "sp")}

        xr, sgS, rtab = m["xn"], m["sgS"], m["rtab"]
        xg, xgT, sg, hh, hT, yy = (m[k] for k in ("xg", "xgT", "sg", "h", "hT", "y"))

        wr_sb = sb("wr_sb", [128, DC, NX])
        tail = [24576]

        def late(n):
            tail[0] += n
            assert tail[0] <= 32768
            return m["arena"][:, tail[0] - n:tail[0]]

        prob, gate, sel, eqs = (late(TT * NX).rearrange("p (t e) -> p t e", t=TT) for _ in range(4))
        selb = sb("selb", [128, TT, NX], BF16)
        part_b = sb("part_b", [128, TT, NX], BF16)

        top8 = sb("top8", [128, TT, 8])
        row1 = sb("row1", [128, 4 * TT])
        rank = late(NX * TT).rearrange("p (e t) -> p e t", t=TT)
        full = late(NX * 10).rearrange("p (e c) -> p e c", c=10)
        tcount = sb("tcount", [128, NX])
        tends = sb("tends", [128, NX])
        tle = sb("tle", [128, 2, NX])
        ttab = sb("ttab", [128, 4])
        ttab_i = sb("ttab_i", [128, 4], I32)
        ends_i = sb("ends_i", [1, NX], I32)
        onehot = late(2 * TT * CAP).bitcast(BF16).rearrange("p (b t h s) -> p b t h s", b=2, t=TT, h=2)
        place_c = sb("place_c", [128, 4])
        idx_t = sb("idx_t", [128, PLACES, 2])
        idx = sb("idx", [128, PLACES], I32)
        gcol = sb("gcol", [128, PLACES])
        tab_d = nc.dram_tensor("tab_d", (136, 4), I32).ap()

        s_wr = sem("s_wr")
        s_var2 = sem("s_var2")
        s_std2 = sem("s_std2")
        s_xr = sem("s_xr")
        s_xrd = sem("s_xrd")
        s_base = sem("s_base")
        s_xrTp = sem("s_xrTp")
        s_xrT = sem("s_xrT")
        s_logit = sem("s_logit")
        s_lmax = sem("s_lmax")
        s_exp = sem("s_exp")
        s_selb = sem("s_selb")
        s_cum = sem("s_cum")
        s_rtab = sem("s_rtab")
        s_tab = sem("s_tab")
        s_tabd = sem("s_tabd")
        s_sw = [sem(f"s_sw{e}") for e in range(NS)]
        s_shG = sem("s_shG")
        s_shU = sem("s_shU")
        s_shsg = sem("s_shsg")
        s_shh = sem("s_shh")
        s_shy = sem("s_shy")
        s_shb = sem("s_shb")
        s_acc = sem("s_acc")
        s_place = sem("s_place")
        s_arr = [sem(f"s_arr{i}") for i in range(RING)]
        s_w = sem("s_w")
        s_hot = sem("s_hot")
        s_look = sem("s_look")
        s_idx0 = sem("s_idx0")
        s_idx1 = sem("s_idx1")
        s_idx = sem("s_idx")
        s_xg = [sem(f"s_xg{b}") for b in range(2)]
        s_xgTp = sem("s_xgTp")
        s_xgT = sem("s_xgT")
        s_G = sem("s_G")
        s_U = sem("s_U")
        s_sg = sem("s_sg")
        s_h = sem("s_h")
        s_hTp = sem("s_hTp")
        s_hT = sem("s_hT")
        s_y = sem("s_y")
        s_ys = sem("s_ys")
        s_scat = [sem(f"s_scat{b}") for b in range(2)]
        s_added = sem("s_added")
        s_out = sem("s_out")



        def hold(eng, who, s, value):
            eng.wait_ge(s, value)
            eng.sem_inc(passed[who], 1)

        chain = [0]

        def then(dve, ins):
            chain[0] += 1
            ins.then_inc(s_dve, 1)
            dve.wait_ge(s_dve, chain[0])

        block = ctx.enter_context(nc.Block())

        @block.sync
        def _(sp):
            sp.dma_start(x_sb[:, :, :], x.rearrange("(t p) d -> p t d", t=TT)).then_inc(s_x, 16)
            for a, e in enumerate((dst, src)):
                sp.dma_start(edge_i[0:ET - 1, a, :], e[0:(ET - 1) * 128].rearrange("(t p) -> t p", p=128)).then_inc(s_edge, 16)
                sp.dma_start(edge_i[ET - 1:ET, a, :], e[LAST_ROW:E].rearrange("(t p) -> t p", p=128)).then_inc(s_edge, 16)
            sp.dma_start(pidx_i, paths.rearrange("(o p) c -> o (p c)", o=1).to_broadcast([128, PATHS * 3])).then_inc(s_path, 16)
            sp.dma_start(coef[:, :], coeffs.rearrange("(o p) -> o p", o=1).to_broadcast([128, PATHS])).then_inc(s_path, 16)
            sp.dma_start(wqkv_sb, wqkv.rearrange("(c p) n -> p c n", p=128)).then_inc(s_wqkv, 16)
            sp.wait_ge(s_rmz, 1)
            sp.dma_start(rm2[0:HD, 0:FD], rm).then_inc(s_rm, 16)
            sp.dma_start(rm2[HD:128, FD:2 * FD], rm).then_inc(s_rm, 16)
            sp.dma_start(wout_sb, wout.rearrange("(c p) n -> p c n", p=128)).then_inc(s_wout, 16)
            sp.dma_start(bout_b, bout.rearrange("(o d) -> o d", o=1).to_broadcast([TR, D])).then_inc(s_bout, 16)
            sp.wait_ge(s_xn, TT)
            sp.dma_start(xn_d.rearrange("(t p) d -> p t d", t=TT), xn).then_inc(s_xnd, 16)
            sp.dma_start(xr_d[N:ROWS, :], zeros_b[0:CAP, :]).then_inc(s_dummy, 16)
            sp.dma_start(acc_d[N:ROWS, :], zeros_b[0:CAP, :]).then_inc(s_dummy, 16)
            sp.wait_ge(s_fldi, 1)
            sp.dma_start(items_d, itemT).then_inc(s_items, 16)
            sp.wait_ge(s_items, 16)
            sp.wait_ge(s_mix, TT)
            sp.wait_ge(s_dummy, 32)
            n_items = sp.value_load(items_row[:, 5 * 896:5 * 896 + 1], min_val=1, max_val=PAIRS)
            rows = [sp.alloc_register(f"sp_row{i}") for i in range(GROUP)]
            with sp.Fori(0, BLOCKS) as blk:
                with sp.If(blk * (DUOS * 16) < n_items):
                    with sp.Fori(0, DUOS) as duo:
                        for b in range(2):
                            g = (blk * DUOS + duo) * 2 + b
                            with sp.If(g * GROUP < n_items):
                                sp.load(rows, items_row[:, bass.ds(2 * 896 + g * GROUP, GROUP)])
                                hold(sp, "sp", s_prod, g * 2 + 2)
                                for i in range(GROUP):
                                    r = sp.snap(rows[i], min_val=0, max_val=LAST_ROW)
                                    sp.dma_start(x2[:, b, i, :], edge[bass.ds(r, 128), :]).then_inc(s_x2[b], 16)
            sp.dma_start(wr_sb[:, :, :], wr.rearrange("(c p) n -> p c n", p=128)).then_inc(s_wr, 16)

            def load_expert(e, slot, gud, s):
                for k, w in enumerate(gud):
                    sp.dma_start(ring[:, slot, k], w[e].rearrange("(c p) n -> p c n", p=128)).then_inc(s, 16)

            sp.wait_ge(s_flushed, 1)
            sp.wait_ge(s_gnn, TT)
            load_expert(0, 2, (swg, swu, swd), s_sw[0])
            load_expert(1, 3, (swg, swu, swd), s_sw[1])
            for e in range(2):
                load_expert(e, e, (wg, wu, wd), s_arr[e])
            sp.wait_ge(s_xr, TT)
            sp.dma_start(xr_d[0:N, :].rearrange("(t p) d -> p t d", t=TT), xr).then_inc(s_xrd, 16)
            sp.wait_ge(s_tab, 1)
            sp.dma_start(tab_d[0:128, :], ttab_i[:, :]).then_inc(s_tabd, 16)
            sp.dma_start(ends_d, ends_i[:, :]).then_inc(s_tabd, 16)
            for e in range(2):
                sp.wait_ge(s_shy, (e + 1) * TT)
                load_expert(e + 2, e + 2, (wg, wu, wd), s_arr[e + 2])
            sp.wait_ge(s_shb, NS * TT)
            sp.dma_start(acc_d[0:N, :].rearrange("(t p) d -> p t d", t=TT), x_sb[:, :, :]).then_inc(s_acc, 16)
            sp.wait_ge(s_tabd, 32)
            sp.wait_ge(s_arr[0], 48)
            sp.sem_inc(s_w, 1)
            with sp.Fori(0, (NX - RING) // RING) as q:
                for r in range(RING):
                    e = q * RING + (r + 1)
                    end = sp.value_load(ends_d[:, bass.ds(e - 1, 1)], min_val=1, max_val=MAX_TILES)
                    hold(sp, "sp", s_arr[(r + 1) % RING], (q + 1 + (r + 1) // RING) * 48)
                    sp.sem_inc(s_w, 1)
                    hold(sp, "sp", s_y, end + 1)
                    load_expert(bass.ds(e + 3, 1) if False else e + 3, r, (wg, wu, wd), s_arr[r])
            for e in range(NX - RING + 1, NX):
                sp.wait_ge(s_arr[e % RING], 48 * (e // RING + 1))
                sp.sem_inc(s_w, 1)

        @block.gpsimd
        def _(pool):
            pool.memset(rm2, 0.0).then_inc(s_rmz, 1)
            pool.memset(zeros_b, 0.0)
            pool.iota(iota[:, :], pattern=[[1, 768]], base=0, channel_multiplier=0, allow_small_or_imprecise_dtypes=True)
            pool.iota(prow[:, :], pattern=[[0, 1]], base=0, channel_multiplier=1, allow_small_or_imprecise_dtypes=True)
            pool.iota(jcol[:, :], pattern=[[128, JC]], base=0, channel_multiplier=1, allow_small_or_imprecise_dtypes=True)
            pool.iota(w64[:, :], pattern=[[W, NW + 2]], base=0, channel_multiplier=0, allow_small_or_imprecise_dtypes=True)
            pool.iota(quad[:, :], pattern=[[32, 5]], base=0, channel_multiplier=0, allow_small_or_imprecise_dtypes=True)
            pool.memset(ones[:, :], 1.0)
            pool.memset(zero_l[:, :], 0.0)
            pool.memset(zero_r[:, :], 0.0)
            pool.memset(eps_c[:, :], EPS).then_inc(s_iota, 1)

            pool.wait_ge(s_items, 16)
            pool.wait_ge(s_xnd, 16)
            pool.wait_ge(s_mix, TT)
            pool.wait_ge(s_edgeS, 1)
            pool.wait_ge(s_ge, 1)
            n_items = pool.value_load(items_row[:, 5 * 896:5 * 896 + 1], min_val=1, max_val=PAIRS)
            tiles = [pool.alloc_register(f"pool_tile{i}") for i in range(GROUP)]
            wins = [pool.alloc_register(f"pool_win{i}") for i in range(GROUP)]
            with pool.Fori(0, BLOCKS) as blk:
                with pool.If(blk * (DUOS * 16) < n_items):
                    with pool.Fori(0, DUOS) as duo:
                        for b in range(2):
                            g = (blk * DUOS + duo) * 2 + b
                            with pool.If(g * GROUP < n_items):
                                pool.load(tiles, items_row[:, bass.ds(3 * 896 + g * GROUP, GROUP)])
                                pool.load(wins, items_row[:, bass.ds(4 * 896 + g * GROUP, GROUP)])
                                hold(pool, "pool", s_prod, g * 2 + 2)
                                for i in range(GROUP):
                                    t = pool.snap(tiles[i], min_val=0, max_val=ET - 1)
                                    w = pool.snap(wins[i], min_val=0, max_val=NW)
                                    s = b * GROUP + i
                                    pool.tensor_tensor(dsel[:, b, i:i + 1], dstT[:, bass.ds(t, 1)], w64[:, bass.ds(w, 1)], ALU.subtract)
                                    sel = pool.tensor_copy(ssel[:, s:s + 1], srcT[:, bass.ds(t, 1)])
                                sel.then_inc(s_sel, 1)
                                hold(pool, "pool", s_sel, g + 1)
                                for i in range(GROUP):
                                    s = b * GROUP + i
                                    pool.indirect_dma_start(x1[:, b, i, :], None, xn_d, bass.IndirectOffsetOnAxis(ap=ssel[:, s:s + 1], axis=0)).then_inc(s_x1[b], 16)
            pool.wait_ge(s_flushed, 1)
            pool.wait_ge(s_pm, 1)
            for k, (i, w) in enumerate(MOVES):
                ins = pool.tensor_scalar(move[:, k, :], iota[:, 0:TR], pm[:, :], float(W * w - TR * i), ALU.subtract, ALU.is_equal)
            ins.then_inc(s_move, 1)
            pool.wait_ge(s_comb, TT)
            for t in range(TT):
                pool.memset(rtab[:, :, t, 0], float(t))
            pool.memset(rtab[:, :, :, 2], 1.0)
            pool.tensor_scalar(rtab[:, :, :, 1], prow[0:TR, :, None].to_broadcast([TR, NX, TT]), 2.0, None, ALU.mult).then_inc(s_place, 1)
            pool.wait_ge(s_tabd, 32)
            pool.wait_ge(s_xrd, 16)
            pool.wait_ge(s_dummy, 32)
            pool.wait_ge(s_acc, 16)

            def gather(u, b, i, n):
                return pool.indirect_dma_start(xg[:, b, :], None, xr_half, bass.IndirectOffsetOnAxis(ap=idx[:, i:i + 1], axis=0)).then_inc(s_xg[b], 16)

            for u in range(3):
                pool.wait_ge(s_idx, u + 1)
                if u == 2:
                    pool.wait_ge(s_xgTp, 1)
                gather(u, u % 2, u, 1)
            n = pool.value_load(tab_d[0:1, 3:4], min_val=MAX_TILES // 2, max_val=MAX_TILES)
            pool.sem_inc(s_added, PLACES)
            with pool.Fori(0, T_BLOCKS) as blk:
                with pool.If(blk * (2 * T_DUOS) < n):
                    with pool.Fori(0, T_DUOS * 2 // PLACES) as part:
                        for r in range(PLACES):
                            u = (blk * (T_DUOS * 2 // PLACES) + part) * PLACES + r
                            with pool.If(u + 3 < n):
                                hold(pool, "pool", s_idx, u + 4)
                                hold(pool, "pool", s_xgTp, u + 2)
                                gather(u + 3, (r + 3) % 2, (r + 3) % PLACES, 1)
                            with pool.If(u < n):
                                hold(pool, "pool", s_ys, u + 2)
                                pool.indirect_dma_start(acc_half, bass.IndirectOffsetOnAxis(ap=idx[:, r:r + 1], axis=0), yy[:, r % 2, :], None,
                                                        compute_op=ALU.add).then_inc(s_scat[r % 2], 16)
                                hold(pool, "pool", s_scat[r % 2], ((blk * (T_DUOS * 2 // PLACES) + part) * (PLACES // 2) + r // 2 + 1) * 16)
                                pool.sem_inc(s_added, 1)
            pool.dma_start(out.rearrange("(p r) d -> p (r d)", p=TR), acc_d[0:N, :].rearrange("(p r) d -> p (r d)", p=TR)).then_inc(s_out, 16)
            pool.wait_ge(s_out, 16)

        @block.scalar
        def _(act):
            act.wait_ge(s_iota, 1)
            act.wait_ge(s_var, 1)
            act.activation(rstd[0:TR, :], mv[0:TR, :, 1], ACT.Sqrt, bias=eps_c[0:TR, :]).then_inc(s_std, 1)
            for t in range(TT):
                act.wait_ge(s_xTp, t + 1)
                act.copy(xT[:, :, t * TR:(t + 1) * TR], bank[2 + t % 2][:, 0:DC * TR].rearrange("p (c n) -> p c n", c=DC)).then_inc(s_xT, 1)
            act.wait_ge(s_cnt, 1)
            act.copy(cnt[:, 0:6, :], bank[0][:, 0:504].rearrange("p (w t) -> p w t", t=ET)).then_inc(s_cnts, 1)
            act.copy(cnt[:, 6:NW + 1, :], bank[1][:, 0:420].rearrange("p (w t) -> p w t", t=ET)).then_inc(s_cnts, 1)
            for c in range(8):
                for h, (a, n) in enumerate(HALVES):
                    act.wait_ge(s_qkp, 2 * c + h + 1)
                    act.copy(qkT[:, c, a:a + n], bank[4 + (2 * c + h) % 4][:, 0:n]).then_inc(s_qk, 1)
            for t in range(TT):
                act.wait_ge(s_vp, t + 1)
                act.copy(v[:, t, :, 0:HD], bank[2 + t % 2][0:TR, :].rearrange("p (h c) -> p h c", h=NH)).then_inc(s_v, 1)
            for g in range(2):
                act.wait_ge(s_qmin, g + 1)
                act.activation(elu_q[:, g, :], elu_q[:, g, :], ACT.Exp).then_inc(s_qexp, 1)
            for t in range(TT):
                act.wait_ge(s_kmin, t + 1)
                act.activation(elu_k[:, t % 2, :], elu_k[:, t % 2, :], ACT.Exp).then_inc(s_kexp, 1)
            for t in range(TT):
                act.wait_ge(s_zTp, t + 1)
                act.copy(zT[:, :, t * TR:(t + 1) * TR], bank[2 + t % 2][:, 0:DC * TR].rearrange("p (c n) -> p c n", c=DC)).then_inc(s_zT, 1)

            act.wait_ge(s_items, 16)
            n_items = act.value_load(items_row[:, 5 * 896:5 * 896 + 1], min_val=1, max_val=PAIRS)
            lasts = [act.alloc_register(f"act_last{i}") for i in range(GROUP)]
            wins = [act.alloc_register(f"act_win{i}") for i in range(GROUP)]
            act.wait_ge(s_zsum, 1)
            act.sem_inc(s_flush[0], 1)
            act.sem_inc(s_flush[1], 1)
            with act.Fori(0, BLOCKS) as blk:
                with act.If(blk * (DUOS * 16) < n_items):
                    with act.Fori(0, DUOS) as duo:
                        for b in range(2):
                            g = (blk * DUOS + duo) * 2 + b
                            with act.If(g * GROUP < n_items):
                                act.load(lasts, items_row[:, bass.ds(1 * 896 + g * GROUP, GROUP)])
                                act.load(wins, items_row[:, bass.ds(4 * 896 + g * GROUP, GROUP)])
                                for h in range(2):
                                    for i in range(GROUP):
                                        last = act.snap(lasts[i], min_val=0, max_val=1)
                                        w = act.snap(wins[i], min_val=0, max_val=NW - 1)
                                        hold(act, "act", s_item[h], g * GROUP + i + 2)
                                        with act.If(last == 1):
                                            act.copy(sums[:, bass.ds(w, 1), h, :], bank[h][:, None, :]).then_inc(s_flush[h], 1)
                                        with act.Else():
                                            act.sem_inc(s_flush[h], 1)
            act.copy(small[0:1, 40:41], eps_c[0:1, :]).then_inc(s_flushed, 1)

            act.wait_ge(s_var2, 1)
            act.activation(rstd[0:TR, :], mv[0:TR, :, 1], ACT.Sqrt, bias=eps_c[0:TR, :]).then_inc(s_std2, 1)
            for t in range(TT):
                act.wait_ge(s_xrTp, t + 1)
                act.copy(xT[:, :, t * TR:(t + 1) * TR], bank[4 + t % 2][:, 0:DC * TR].rearrange("p (c n) -> p c n", c=DC)).then_inc(s_xrT, 1)
            act.wait_ge(s_lmax, 1)
            act.activation(prob[0:TR, :, :], prob[0:TR, :, :], ACT.Exp).then_inc(s_exp, 1)
            for e in range(NS):
                for h, (a, nn) in enumerate(HALVES):
                    for c in range(DC):
                        u = (e * 2 + h) * DC + c
                        act.wait_ge(s_shG, u + 1)
                        if u >= 2:
                            act.wait_ge(s_shh, u - 1)
                        act.activation(sgS[:, u % 2, 0:nn], bank[3 + 2 * (u % 2)][:, 0:nn], ACT.Silu).then_inc(s_shsg, 1)

            def xgT_copy(b):
                return act.copy(xgT[:, b, :], bank[1][:, 0:2 * 128]).then_inc(s_xgT, 1)

            def silu(b):
                return act.activation(sg[:, b, :], bank[3 + 2 * b][:, 0:HF], ACT.Silu).then_inc(s_sg, 1)

            for u in range(2):
                act.wait_ge(s_xgTp, u + 1)
                xgT_copy(u)
            act.wait_ge(s_G, 1)
            silu(0)
            act.wait_ge(s_tabd, 32)
            act.sem_inc(s_ys, 1)
            n = act.value_load(tab_d[0:1, 3:4], min_val=MAX_TILES // 2, max_val=MAX_TILES)
            with act.Fori(0, T_BLOCKS) as blk:
                with act.If(blk * (2 * T_DUOS) < n):
                    with act.Fori(0, T_DUOS * 2 // PLACES) as part:
                        for r in range(PLACES):
                            u = (blk * (T_DUOS * 2 // PLACES) + part) * PLACES + r
                            b = r % 2
                            with act.If(u < n):
                                act.wait_ge(s_hTp, u + 1)
                                act.copy(hT[:, b, :], bank[2][:, 0:2 * 128]).then_inc(s_hT, 1)
                            with act.If(u + 2 < n):
                                act.wait_ge(s_xgTp, u + 3)
                                xgT_copy(b)
                            with act.If(u + 1 < n):
                                act.wait_ge(s_G, u + 2)
                                silu(1 - b)
                            with act.If(u < n):
                                hold(act, "act", s_added, u + PLACES - 1)
                                act.wait_ge(s_y, u + 2)
                                act.activation(yy[:, b, :], bank[7][:, 0:HF], ACT.Copy, scale=gcol[:, r:r + 1]).then_inc(s_ys, 1)

        @block.vector
        def _(dve):
            dve.wait_ge(s_iota, 1)
            dve.tensor_scalar(ident[:, :], iota[:, 0:128], prow[:, :], None, ALU.is_equal)
            dve.tensor_scalar(tri[:, :], iota[:, 0:128], prow[:, :], None, ALU.is_ge)
            dve.tensor_scalar(place[:, 0:1], prow[:, :], float(N), None, ALU.add)
            dve.tensor_scalar(place[:, 1:2], prow[:, :], float(N), -1.0, ALU.add, ALU.mult)
            then(dve, dve.tensor_scalar(quad[:, :], quad[:, :], prow[:, :], None, ALU.is_le))
            then(dve, dve.tensor_scalar(small[:, 1:2], quad[:, 2:3], float(-W), None, ALU.mult))
            dve.tensor_tensor(pm[:, :], small[:, 1:2], prow[:, :], ALU.add).then_inc(s_pm, 1)
            dve.tensor_tensor(qmask[:, :], quad[:, 0:4], quad[:, 1:5], ALU.subtract).then_inc(s_const, 1)
            dve.wait_ge(s_edge, 64)
            dve.tensor_copy(edge_f[:, :, :], edge_i[:, :, :]).then_inc(s_edgef, 1)
            dve.wait_ge(s_x, 16)
            for t in range(TT):
                ins = dve.bn_stats(stats[0:TR, t, :], x_sb[:, t, :])
            then(dve, ins)
            for t in range(TT):
                ins = dve.bn_aggr(mv[0:TR, t, :], stats[0:TR, t, :])
            ins.then_inc(s_var, 1)
            dve.wait_ge(s_std, 1)
            then(dve, dve.reciprocal(rstd[0:TR, :], rstd[0:TR, :]))
            dve.wait_ge(s_var, 1)
            for t in range(TT):
                dve.tensor_scalar(xn[:, t, :], x_sb[:, t, :], mv[0:TR, t, 0:1], rstd[0:TR, t:t + 1], ALU.subtract, ALU.mult).then_inc(s_xn, 1)
            dve.wait_ge(s_edgeT, 1)
            dve.tensor_copy(srcT[:, :], bank[0][:, 128:128 + ET]).then_inc(s_edgeS, 1)
            then(dve, dve.tensor_copy(dstT[:, :], bank[0][:, 0:ET]))
            then(dve, dve.tensor_scalar(small[:, 0:1], prow[:, :], float(ET * 128 - E), None, ALU.is_ge))
            then(dve, dve.tensor_scalar(dstT[:, ET - 1:ET], dstT[:, ET - 1:ET], 1.0, small[:, 0:1], ALU.add, ALU.mult))
            then(dve, dve.tensor_scalar(dstT[:, ET - 1:ET], dstT[:, ET - 1:ET], -1.0, None, ALU.add))
            dve.tensor_tensor(ge[:, :, :], dstT[:, None, :].to_broadcast([128, NW + 1, ET]),
                              w64[:, 0:NW + 1, None].to_broadcast([128, NW + 1, ET]), ALU.is_ge).then_inc(s_ge, 1)
            dve.wait_ge(s_path, 32)
            dve.tensor_scalar(poff[0:1, :].rearrange("p (k c) -> p k c", c=2),
                              pidx_i[0:1, :].rearrange("p (k c) -> p k c", c=3)[:, :, 0:2], float(EXT), None, ALU.mult).then_inc(s_poff, 1)
            dve.tensor_scalar(toff[0:1, :], pidx_i[0:1, :].rearrange("p (k c) -> p k c", c=3)[:, :, 2], float(EXT), None, ALU.mult).then_inc(s_poff, 1)
            dve.wait_ge(s_cnts, 2)
            then(dve, dve.tensor_tensor(active.rearrange("p (w t) -> p w t", t=ET), cnt[:, 0:NW, :], cnt[:, 1:NW + 1, :], ALU.not_equal))
            then(dve, dve.tensor_tensor_scan(upto, active, active, 0.0, ALU.add, ALU.bypass))
            for c in range(JC):
                then(dve, dve.tensor_scalar(junk, upto, jcol[:, c:c + 1], 0.0, ALU.is_le, ALU.add, accum_out=qj[:, c:c + 1]))
            for a in range(3):
                dve.tensor_scalar(j3[:, a, :], jcol[:, :], float(a - 1), None, ALU.add)
            then(dve, dve.tensor_copy(fld[:, 5, :], upto[:, PAIRS - 1:PAIRS].to_broadcast([128, JC])))
            ends = upto.rearrange("p (w t) -> p w t", t=ET)[:, :, ET - 1]
            for a in range(3):
                ins = dve.tensor_tensor(wcmp[:, a], j3[:, a, :, None].to_broadcast([128, JC, NW]),
                                        ends[:, None, :].to_broadcast([128, JC, NW]), ALU.is_ge)
            then(dve, ins)
            then(dve, dve.tensor_reduce(wj, wcmp, AX, ALU.add))
            dve.tensor_copy(fld[:, 4, :], wj[:, 1, :])
            then(dve, dve.tensor_scalar(small[:, 8:8 + JC], jcol[:, :], 0.0, None, ALU.is_equal))
            then(dve, dve.tensor_tensor(wj[:, 0, :], wj[:, 0, :], small[:, 8:8 + JC], ALU.subtract))
            dve.tensor_tensor(fld[:, 0, :], wj[:, 1, :], wj[:, 0, :], ALU.not_equal)
            dve.tensor_tensor(fld[:, 1, :], wj[:, 1, :], wj[:, 2, :], ALU.not_equal)
            then(dve, dve.scalar_tensor_tensor(fld[:, 3, :], wj[:, 1, :], -float(ET), qj, ALU.mult, ALU.add))
            dve.tensor_scalar(fld[:, 2, :], fld[:, 3, :], 128.0, float(LAST_ROW), ALU.mult, ALU.min).then_inc(s_fld, 1)
            dve.wait_ge(s_fldT, 1)
            dve.tensor_copy(itemT, bank[0][0:FIELDS * JC, 256:384]).then_inc(s_fldi, 1)
            dve.memset(v[:, :, :, HD:HD + 1], 1.0).then_inc(s_v, 1)
            for g in range(2):
                for h, (a, n) in enumerate(HALVES):
                    dve.wait_ge(s_qfp, 2 * g + h + 1)
                    ins = dve.tensor_scalar(elu_q[:, g, a:a + n], bank[2 * g + h][:, 0:n], 0.0, None, ALU.min)
                ins.then_inc(s_qmin, 1)
                dve.wait_ge(s_qexp, g + 1)
                for h, (a, n) in enumerate(HALVES):
                    dve.scalar_tensor_tensor(qp[:, g, a:a + n], bank[2 * g + h][:, 0:n], 0.0, elu_q[:, g, a:a + n], ALU.max, ALU.add).then_inc(s_q, 1)
            for t in range(TT):
                dve.wait_ge(s_kfp, t + 1)
                dve.tensor_scalar(elu_k[:, t % 2, :], bank[4 + t % 2][0:TR, 0:256], 0.0, None, ALU.min).then_inc(s_kmin, 1)
                dve.wait_ge(s_kexp, t + 1)
                dve.scalar_tensor_tensor(kp[:, t, :], bank[4 + t % 2][0:TR, 0:256], 0.0, elu_k[:, t % 2, :], ALU.max, ALU.add).then_inc(s_k, 1)
            for g in range(2):
                dve.wait_ge(s_kvp, g + 1)
                dve.tensor_tensor(kvm[:, g], bank[6 + g][:, 0:260].rearrange("p (h c) -> p h c", h=4),
                                  qmask[:, :, None].to_broadcast([128, 4, HD + 1]), ALU.mult).then_inc(s_kv, 1)
            for t in range(TT):
                for g in range(2):
                    zb = bank[4 * (t % 2) + g if t % 2 == 0 else 4 + g][0:TR, 0:260].rearrange("p (h c) -> p h c", h=4)
                    dve.wait_ge(s_zp, 2 * t + g + 1)
                    then(dve, dve.tensor_scalar(recip2[:, t, 4 * g:4 * g + 4], zb[:, :, HD], 1e-6, None, ALU.add))
                    then(dve, dve.reciprocal(recip[:, t, 4 * g:4 * g + 4], recip2[:, t, 4 * g:4 * g + 4]))
                    dve.tensor_tensor(z[:, t, 256 * g:256 * g + 256].rearrange("p (h c) -> p h c", h=4), zb[:, :, 0:HD],
                                      recip[:, t, 4 * g:4 * g + 4, None].to_broadcast([TR, 4, HD]), ALU.mult).then_inc(s_z, 1)
            dve.wait_ge(s_bout, 16)
            for t in range(TT):
                then(dve, dve.tensor_tensor(x_sb[:, t, :], x_sb[:, t, :], bout_b, ALU.add))
            for t in range(TT):
                dve.wait_ge(s_mixp, t + 1)
                dve.tensor_tensor(x_sb[:, t, :], x_sb[:, t, :], bank[t % 2][0:TR, :], ALU.add).then_inc(s_mix, 1)

            dve.wait_ge(s_xnd, 16)
            dve.memset(m["low"][:, :], 0.0).then_inc(s_zsum, 1)
            dve.wait_ge(s_items, 16)
            dve.wait_ge(s_mix, TT)
            n_items = dve.value_load(items_row[:, 5 * 896:5 * 896 + 1], min_val=1, max_val=PAIRS)
            offs = [dve.alloc_register(f"dve_off{i}") for i in range(16)]
            dve.wait_ge(s_poff, 2)
            dve.sem_inc(s_prod, 4)
            with dve.Fori(0, BLOCKS) as blk:
                with dve.If(blk * (DUOS * 16) < n_items):
                    with dve.Fori(0, DUOS) as duo:
                        for b in range(2):
                            g = (blk * DUOS + duo) * 2 + b
                            with dve.If(g * GROUP < n_items):
                                dve.wait_ge(s_sel, g + 1)
                                dve.tensor_tensor(pair[:, b, :, :], iota[:, None, 0:W].to_broadcast([128, GROUP, W]),
                                                  dsel[:, b, :, None].to_broadcast([128, GROUP, W]), ALU.is_equal)
                                for h in range(2):
                                    for p in range(PH):
                                        path = h * PH + p
                                        if p % 8 == 0:
                                            dve.load(offs, poff[0:1, 2 * path:2 * path + 16])
                                        i1 = dve.snap(offs[2 * (p % 8)], min_val=0, max_val=D - EXT)
                                        i2 = dve.snap(offs[2 * (p % 8) + 1], min_val=0, max_val=D - EXT)
                                        if p == 0:
                                            hold(dve, "dve", s_item[h], g * GROUP + 1)
                                            if h == 0:
                                                hold(dve, "dve", s_x1[b], (blk * DUOS + duo + 1) * (16 * GROUP))
                                                hold(dve, "dve", s_x2[b], (blk * DUOS + duo + 1) * (16 * GROUP))
                                        ins = dve.tensor_tensor(prod[:, h, :, EXT * p:EXT * p + EXT],
                                                                x1[:, b, :, bass.ds(i1, EXT)], x2[:, b, :, bass.ds(i2, EXT)], ALU.mult)
                                    ins.then_inc(s_prod, 1)
            dve.wait_ge(s_flushed, 1)
            then(dve, dve.memset(node[:, :, :], 0.0))
            for q in range(PATHS // 4):
                if q % 16 == 0:
                    toffs = [dve.alloc_register(f"dve_toff{i}") for i in range(4)]
                for c, r in enumerate(toffs):
                    dve.load([r], toff[0:1, 16 * c + q:16 * c + q + 1])
                for c in range(NCHUNK):
                    i3 = dve.snap(toffs[c], min_val=0, max_val=D - EXT)
                    part = slice(64 * (c % 2), 64 * (c % 2) + 64)
                    path = 16 * c + q
                    seg = node[part, :, bass.ds(i3, EXT)]
                    dve.wait_ge(s_dve, chain[0])
                    chain[0] += 1
                    dve.scalar_tensor_tensor(seg, sums[part, :, c // 2, EXT * q:EXT * q + EXT], coef[part, path:path + 1], seg,
                                             ALU.mult, ALU.add).then_inc(s_dve, 1)
            dve.wait_ge(s_dve, chain[0])
            dve.sem_inc(s_R, 1)
            for t in range(TT):
                dve.wait_ge(s_comb, t + 1)
                dve.tensor_tensor(x_sb[:, t, :], x_sb[:, t, :], bank[2 + t % 2][0:TR, :], ALU.add).then_inc(s_gnn, 1)

            dve.wait_ge(s_gnn, TT)
            for t in range(TT):
                ins = dve.bn_stats(stats[0:TR, t, :], x_sb[:, t, :])
            then(dve, ins)
            for t in range(TT):
                ins = dve.bn_aggr(mv[0:TR, t, :], stats[0:TR, t, :])
            ins.then_inc(s_var2, 1)
            dve.wait_ge(s_std2, 1)
            then(dve, dve.reciprocal(rstd[0:TR, :], rstd[0:TR, :]))
            dve.wait_ge(s_var2, 1)
            for t in range(TT):
                dve.tensor_scalar(xr[:, t, :], x_sb[:, t, :], mv[0:TR, t, 0:1], rstd[0:TR, t:t + 1], ALU.subtract, ALU.mult).then_inc(s_xr, 1)
            dve.wait_ge(s_xr, TT)
            then(dve, dve.tensor_tensor(x_sb[:, :, :], x_sb[:, :, :], xr, ALU.add))

            P5 = prob[0:TR, :, :]
            r1 = row1[0:TR, :].rearrange("p (a t) -> p a t", a=4)

            def wide(col):
                return col[:, :, None].to_broadcast([TR, TT, NX])

            dve.wait_ge(s_logit, 1)
            L5 = bank[0][0:TR, 0:TT * NX].rearrange("p (t e) -> p t e", t=TT)
            then(dve, dve.tensor_reduce(r1[:, 0], L5, AX, ALU.max))
            dve.tensor_tensor(P5, L5, wide(r1[:, 0]), ALU.subtract).then_inc(s_lmax, 1)
            dve.wait_ge(s_exp, 1)
            then(dve, dve.tensor_reduce(r1[:, 1], P5, AX, ALU.add))
            then(dve, dve.reciprocal(r1[:, 2], r1[:, 1]))
            then(dve, dve.tensor_tensor(P5, P5, wide(r1[:, 2]), ALU.mult))
            for t in range(TT):
                ins = dve.max(top8[0:TR, t, :], prob[0:TR, t, :])
            then(dve, ins)
            sixth = top8[0:TR, :, TOPK - 1:TOPK].to_broadcast([TR, TT, NX])
            S5, E5, G5 = sel[0:TR], eqs[0:TR], gate[0:TR]
            dve.tensor_tensor(S5, P5, sixth, ALU.is_gt)
            then(dve, dve.tensor_tensor(E5, P5, sixth, ALU.is_equal))
            then(dve, dve.tensor_reduce(r1[:, 0], S5, AX, ALU.add))
            for t in range(TT):
                ins = dve.tensor_tensor_scan(gate[0:TR, t, :], eqs[0:TR, t, :], eqs[0:TR, t, :], 0.0, ALU.add, ALU.bypass)
            then(dve, ins)
            then(dve, dve.tensor_tensor(G5, G5, wide(r1[:, 0]), ALU.add))
            then(dve, dve.scalar_tensor_tensor(E5, G5, float(TOPK), E5, ALU.is_le, ALU.mult))
            then(dve, dve.tensor_tensor(S5, S5, E5, ALU.add))
            dve.tensor_copy(selb[0:TR], S5).then_inc(s_selb, 1)
            then(dve, dve.tensor_tensor(G5, P5, S5, ALU.mult))
            then(dve, dve.tensor_reduce(r1[:, 1], G5, AX, ALU.add))
            then(dve, dve.reciprocal(r1[:, 2], r1[:, 1]))
            then(dve, dve.tensor_tensor(G5, G5, wide(r1[:, 2]), ALU.mult))
            for k in range(3):
                tcol = rtab[:, :, :, 3 + k].rearrange("p e t -> p t e")
                then(dve, dve.tensor_copy(part_b[0:TR], G5))
                dve.tensor_copy(tcol, part_b[0:TR])
                then(dve, dve.tensor_tensor(G5, G5, part_b[0:TR], ALU.subtract))
            dve.sem_inc(s_rtab, 1)
            dve.wait_ge(s_cum, 1)
            then(dve, dve.tensor_tensor(E5, bank[1][0:TR, 0:TT * NX].rearrange("p (t e) -> p t e", t=TT), S5, ALU.mult))
            then(dve, dve.tensor_scalar(rank[0:TR].rearrange("p e t -> p t e"), E5, -1.0, None, ALU.add))
            then(dve, dve.tensor_tensor(full[:, :, :], bank[2][:, 0:NX, None].to_broadcast([128, NX, 10]),
                                        w64[:, None, 0:10].to_broadcast([128, NX, 10]), ALU.is_gt))
            then(dve, dve.tensor_reduce(tcount[:, :], full[:, :, :], AX, ALU.add))
            then(dve, dve.tensor_tensor_scan(tends[:, :], tcount[:, :], tcount[:, :], 0.0, ALU.add, ALU.bypass))
            dve.tensor_copy(ends_i[:, :], tends[0:1, :])
            then(dve, dve.tensor_scalar(tle[:, 0, :], tends[:, :], prow[:, :], None, ALU.is_le))
            then(dve, dve.tensor_tensor(tle[:, 1, :], tle[:, 0, :], tcount[:, :], ALU.mult))
            then(dve, dve.tensor_reduce(ttab[:, 0:2], tle[:, :, :], AX, ALU.add))
            then(dve, dve.tensor_scalar(ttab[:, 0:1], ttab[:, 0:1], float(NX - 1), None, ALU.min))
            then(dve, dve.tensor_scalar(ttab[:, 1:2], ttab[:, 1:2], prow[:, :], -float(CAP), ALU.subtract, ALU.mult))
            then(dve, dve.tensor_copy(ttab[:, 2:4], tends[:, NX - 1:NX].to_broadcast([128, 2])))
            then(dve, dve.tensor_copy(ttab_i[:, :], ttab[:, :]))
            dve.sem_inc(s_tab, 1)
            then(dve, dve.tensor_scalar(place_c[:, 0:1], prow[:, :], float(CAP), None, ALU.is_ge))
            then(dve, dve.tensor_scalar(place_c[:, 3:4], pm[:, :], 2.0, 2.0 * N, ALU.mult, ALU.add))
            then(dve, dve.tensor_tensor(place_c[:, 1:2], place_c[:, 3:4], place_c[:, 0:1], ALU.add))
            then(dve, dve.tensor_tensor(place_c[:, 2:3], place_c[:, 0:1], place_c[:, 1:2], ALU.subtract))

            for e in range(NS):
                for h, (a, nn) in enumerate(HALVES):
                    for c in range(DC):
                        u = (e * 2 + h) * DC + c
                        dve.wait_ge(s_shsg, u + 1)
                        dve.wait_ge(s_shU, u + 1)
                        if e > 0 and u % 8 == 0:
                            dve.wait_ge(s_shy, e * TT)
                        dve.tensor_tensor(hS[:, c, a:a + nn], sgS[:, u % 2, 0:nn], bank[4 + 2 * (u % 2)][:, 0:nn], ALU.mult).then_inc(s_shh, 1)
                for t in range(TT):
                    dve.wait_ge(s_shy, e * TT + t + 1)
                    if e > 0:
                        dve.wait_ge(s_shb, (e - 1) * TT + t + 1)
                    dve.tensor_tensor(x_sb[:, t, :], x_sb[:, t, :], bank[1 if t % 2 else 7][0:TR, :], ALU.add).then_inc(s_shb, 1)

            dve.wait_ge(s_tabd, 32)

            def one_hot(u, b):
                e = dve.value_load(tab_d[u:u + 1, 0:1] if isinstance(u, int) else tab_d[bass.ds(u, 1), 0:1], min_val=0, max_val=NX - 1)
                base = dve.value_load(tab_d[u:u + 1, 1:2] if isinstance(u, int) else tab_d[bass.ds(u, 1), 1:2], min_val=0, max_val=9 * CAP)
                rk = rank[0:TR, bass.ds(e, 1), :].rearrange("p e t -> p (e t)")
                return dve.tensor_tensor(onehot[0:TR, b], iota[0:TR, None, None, bass.ds(base, CAP)].to_broadcast([TR, TT, 2, CAP]),
                                         rk[:, :, None, None].to_broadcast([TR, TT, 2, CAP]), ALU.is_equal)

            def index(i, wait_1, wait_2):
                look = bank[0][:, 384:390]
                t0 = idx_t[:, i, 0:1]
                t1 = idx_t[:, i, 1:2]
                dve.tensor_reduce(gcol[:, i:i + 1], look[:, 3:6], AX, ALU.add)
                dve.tensor_scalar(t0, look[:, 2:3], place_c[:, 2:3], place_c[:, 1:2], ALU.mult, ALU.add).then_inc(s_idx0, 1)
                dve.wait_ge(s_idx0, wait_1)
                dve.scalar_tensor_tensor(t1, look[:, 0:1], 2.0 * TR, t0, ALU.mult, ALU.add).then_inc(s_idx1, 1)
                dve.wait_ge(s_idx1, wait_2)
                dve.tensor_tensor(idx[:, i:i + 1], look[:, 1:2], t1, ALU.add).then_inc(s_idx, 1)

            def h_mult(b):
                return dve.tensor_tensor(hh[:, b, :], sg[:, b, :], bank[4 + 2 * b][:, 0:HF], ALU.mult).then_inc(s_h, 1)

            for u in range(3):
                if u >= 2:
                    dve.wait_ge(s_look, u - 1)
                one_hot(u, u % 2).then_inc(s_hot, 1)
                dve.wait_ge(s_look, u + 1)
                index(u, u + 1, u + 1)
            one_hot(3, 1).then_inc(s_hot, 1)
            dve.wait_ge(s_sg, 1)
            dve.wait_ge(s_U, 1)
            h_mult(0)
            n = dve.value_load(tab_d[0:1, 3:4], min_val=MAX_TILES // 2, max_val=MAX_TILES)
            with dve.Fori(0, T_BLOCKS) as blk:
                with dve.If(blk * (2 * T_DUOS) < n):
                    with dve.Fori(0, T_DUOS * 2 // PLACES) as part:
                        for r in range(PLACES):
                            u = (blk * (T_DUOS * 2 // PLACES) + part) * PLACES + r
                            b = r % 2
                            with dve.If(u + 3 < n):
                                hold(dve, "dve", s_look, u + 4)
                                hold(dve, "dve", s_added, u + 4)
                                index((r + 3) % PLACES, u + 4, u + 4)
                            with dve.If(u + 4 < n):
                                one_hot(u + 4, b).then_inc(s_hot, 1)
                            with dve.If(u + 1 < n):
                                hold(dve, "dve", s_U, u + 2)
                                hold(dve, "dve", s_hTp, u + 1)
                                dve.wait_ge(s_sg, u + 2)
                                h_mult(1 - b)

        @block.tensor
        def _(pe):
            pe.wait_ge(s_edgef, 1)
            pe.wait_ge(s_const, 1)
            pe.transpose(bank[0][:, 0:ET], edge_f[:, 0, :], ident[0:ET, 0:ET])
            pe.transpose(bank[0][:, 128:128 + ET], edge_f[:, 1, :], ident[0:ET, 0:ET]).then_inc(s_edgeT, 1)
            for t in range(TT):
                pe.wait_ge(s_xn, t + 1)
                if t >= 2:
                    pe.wait_ge(s_xT, t - 1)
                for c in range(DC):
                    ins = pe.transpose(bank[2 + t % 2][:, c * TR:(c + 1) * TR], xn[:, t, c * 128:(c + 1) * 128], ident[0:TR, 0:TR])
                ins.then_inc(s_xTp, 1)
            pe.wait_ge(s_ge, 1)
            pe.matmul(bank[0][:, 0:504], ones[:, :], ge[:, 0:6, :], start=True, stop=True)
            pe.matmul(bank[1][:, 0:420], ones[:, :], ge[:, 6:NW + 1, :], start=True, stop=True).then_inc(s_cnt, 1)
            pe.wait_ge(s_wqkv, 16)
            pe.wait_ge(s_xT, TT)
            for c in range(8):
                for h, (a, n) in enumerate(HALVES):
                    u = 2 * c + h
                    if u >= 4:
                        pe.wait_ge(s_qk, u - 3)
                    for k in range(DC):
                        ins = pe.matmul(bank[4 + u % 4][:, 0:n], wqkv_sb[:, k, c * 128:(c + 1) * 128], xT[:, k, a:a + n],
                                        start=(k == 0), stop=(k == DC - 1))
                    ins.then_inc(s_qkp, 1)
            for t in range(TT):
                if t >= 2:
                    pe.wait_ge(s_v, t - 1)
                for k in range(DC):
                    ins = pe.matmul(bank[2 + t % 2][0:TR, :], xT[:, k, t * TR:(t + 1) * TR], wqkv_sb[:, k, 2 * D:3 * D],
                                    start=(k == 0), stop=(k == DC - 1))
                ins.then_inc(s_vp, 1)
            pe.wait_ge(s_fld, 1)
            pe.transpose(bank[0][0:FIELDS * JC, 256:384], fld.rearrange("p f c -> p (f c)"), ident[:, :]).then_inc(s_fldT, 1)
            pe.wait_ge(s_fldi, 1)
            pe.wait_ge(s_rm, 32)
            pe.wait_ge(s_qk, 16)
            pe.wait_ge(s_v, TT + 1)
            for g in range(2):
                for h, (a, n) in enumerate(HALVES):
                    for hp in range(2):
                        ins = pe.matmul(bank[2 * g + h][64 * hp:64 * hp + 64, 0:n], rm2, qkT[:, 2 * g + hp, a:a + n], start=True, stop=True)
                    ins.then_inc(s_qfp, 1)
            for t in range(TT):
                if t >= 2:
                    pe.wait_ge(s_k, t - 1)
                for c in range(4):
                    ins = pe.matmul(bank[4 + t % 2][0:TR, 64 * c:64 * c + 64], qkT[:, 4 + c, t * TR:(t + 1) * TR], rm2, start=True, stop=True)
                ins.then_inc(s_kfp, 1)
            pe.wait_ge(s_k, TT)
            for g in range(2):
                for t in range(TT):
                    ins = pe.matmul(bank[6 + g][:, 0:260], kp[:, t, 128 * g:128 * g + 128],
                                    v[:, t, 4 * g:4 * g + 4, :], start=(t == 0), stop=(t == TT - 1))
                ins.then_inc(s_kvp, 1)
            pe.wait_ge(s_q, 4)
            for t in range(TT):
                for g in range(2):
                    if t == 0:
                        pe.wait_ge(s_kv, g + 1)
                    if t >= 2:
                        pe.wait_ge(s_z, 2 * (t - 2) + g + 1)
                    pe.matmul(bank[4 * (t % 2) + g][0:TR, 0:260], qp[:, g, t * TR:(t + 1) * TR],
                              kvm[:, g], start=True, stop=True).then_inc(s_zp, 1)
            for t in range(TT):
                pe.wait_ge(s_z, 2 * t + 2)
                if t >= 2:
                    pe.wait_ge(s_zT, t - 1)
                for c in range(DC):
                    ins = pe.transpose(bank[2 + t % 2][:, c * TR:(c + 1) * TR], z[:, t, c * 128:(c + 1) * 128], ident[0:TR, 0:TR])
                ins.then_inc(s_zTp, 1)
            pe.wait_ge(s_wout, 16)
            for t in range(TT):
                pe.wait_ge(s_zT, t + 1)
                if t >= 2:
                    pe.wait_ge(s_mix, t - 1)
                for k in range(DC):
                    ins = pe.matmul(bank[t % 2][0:TR, :], zT[:, k, t * TR:(t + 1) * TR], wout_sb[:, k, :],
                                    start=(k == 0), stop=(k == DC - 1))
                ins.then_inc(s_mixp, 1)

            pe.wait_ge(s_mix, TT)
            pe.wait_ge(s_items, 16)
            n_items = pe.value_load(items_row[:, 5 * 896:5 * 896 + 1], min_val=1, max_val=PAIRS)
            firsts = [pe.alloc_register(f"pe_first{i}") for i in range(GROUP)]
            pe.sem_inc(s_item[0], 1)
            pe.sem_inc(s_item[1], 1)
            with pe.Fori(0, BLOCKS) as blk:
                with pe.If(blk * (DUOS * 16) < n_items):
                    with pe.Fori(0, DUOS) as duo:
                        for b in range(2):
                            g = (blk * DUOS + duo) * 2 + b
                            with pe.If(g * GROUP < n_items):
                                pe.load(firsts, items_row[:, bass.ds(g * GROUP, GROUP)])
                                for h in range(2):
                                    hold(pe, "pe", s_prod, g * 2 + 5 + h)
                                    for i in range(GROUP):
                                        first = pe.snap(firsts[i], min_val=0, max_val=1)
                                        with pe.If(first == 1):
                                            hold(pe, "pe", s_flush[h], g * GROUP + i + 1)
                                            pe.matmul(bank[h][:, :], zero_l[:, :], zero_r[:, :], start=True, stop=False, skip_group_check=True)
                                        for c in range(2):
                                            ins = pe.matmul(bank[h][64 * c:64 * c + 64, :], pair[:, b, i, :],
                                                            prod[:, h, i, 512 * c:512 * c + 512],
                                                            start=False, stop=False, skip_group_check=True)
                                        ins.then_inc(s_item[h], 1)
            pe.wait_ge(s_R, 1)
            pe.wait_ge(s_move, 1)
            for t in range(TT):
                if t >= 2:
                    pe.wait_ge(s_gnn, t - 1)
                mine = [(k, w) for k, (i, w) in enumerate(MOVES) if i == t]
                for k, w in mine:
                    ins = pe.matmul(bank[2 + t % 2][0:TR, :], move[:, k, :], node[:, w, :],
                                    start=(k == mine[0][0]), stop=(k == mine[-1][0]))
                ins.then_inc(s_comb, 1)

            for t in range(TT):
                pe.wait_ge(s_xr, t + 1)
                if t >= 2:
                    pe.wait_ge(s_xrT, t - 1)
                for c in range(DC):
                    ins = pe.transpose(bank[4 + t % 2][:, c * TR:(c + 1) * TR], xr[:, t, c * 128:(c + 1) * 128], ident[0:TR, 0:TR])
                ins.then_inc(s_xrTp, 1)
            pe.wait_ge(s_wr, 16)
            for t in range(TT):
                pe.wait_ge(s_xrT, t + 1)
                for k in range(DC):
                    ins = pe.matmul(bank[0][0:TR, t * NX:(t + 1) * NX], xT[:, k, t * TR:(t + 1) * TR], wr_sb[:, k, :],
                                    start=(k == 0), stop=(k == DC - 1))
            ins.then_inc(s_logit, 1)

            def shared_up(e):
                pe.wait_ge(s_sw[e], 48)
                for h, (a, nn) in enumerate(HALVES):
                    for c in range(DC):
                        u = (e * 2 + h) * DC + c
                        if u >= 2:
                            pe.wait_ge(s_shh, u - 1)
                        for w, s in ((0, s_shG), (1, s_shU)):
                            for k in range(DC):
                                ins = pe.matmul(bank[3 + w + 2 * (u % 2)][:, 0:nn], ring[:, 2 + e, w, k, c * 128:(c + 1) * 128],
                                                xT[:, k, a:a + nn], start=(k == 0), stop=(k == DC - 1))
                            ins.then_inc(s, 1)

            def shared_down(e):
                pe.wait_ge(s_shh, (e + 1) * 2 * DC)
                for t in range(TT):
                    if e * TT + t >= 2:
                        pe.wait_ge(s_shb, e * TT + t - 1)
                    for k in range(DC):
                        ins = pe.matmul(bank[1 if t % 2 else 7][0:TR, :], hS[:, k, t * TR:(t + 1) * TR], ring[:, 2 + e, 2, k, :],
                                        start=(k == 0), stop=(k == DC - 1))
                    ins.then_inc(s_shy, 1)

            pe.wait_ge(s_selb, 1)
            for t in range(TT):
                for i in range(t + 1):
                    pe.matmul(bank[1][0:TR, t * NX:(t + 1) * NX], (tri if i == t else ones)[0:TR, 0:TR], selb[0:TR, i, :],
                              start=(i == 0), stop=(i == t))
            for t in range(TT):
                ins = pe.matmul(bank[2][:, 0:NX], ones[0:TR, :], selb[0:TR, t, :], start=(t == 0), stop=(t == TT - 1))
            ins.then_inc(s_cum, 1)
            pe.wait_ge(s_tab, 1)
            for e in range(NS):
                shared_up(e)
                shared_down(e)

            def lookup(u, b):
                e = pe.value_load(tab_d[u:u + 1, 0:1] if isinstance(u, int) else tab_d[bass.ds(u, 1), 0:1], min_val=0, max_val=NX - 1)
                if isinstance(u, int):
                    pe.wait_ge(s_hot, u + 1)
                    if u >= 1:
                        pe.wait_ge(s_idx, u)
                else:
                    hold(pe, "pe", s_hot, u + 1)
                    hold(pe, "pe", s_idx, u)
                for t in range(TT):
                    ins = pe.matmul(bank[0][:, 384:390], onehot[0:TR, b, t].rearrange("p h s -> p (h s)"),
                                    rtab[:, bass.ds(e, 1), t, :].rearrange("p e c -> p (e c)"), start=(t == 0), stop=(t == TT - 1))
                ins.then_inc(s_look, 1)

            def xg_transpose(b):
                for c in range(2):
                    ins = pe.transpose(bank[1][:, c * 128:(c + 1) * 128], xg[:, b, c * 128:(c + 1) * 128], ident[:, :])
                ins.then_inc(s_xgTp, 1)

            def halves(out_bank, tokT, b, w, slot, s):
                for k in range(DC):
                    lhs = tokT[:, b, 128 * (k % 2) + 64 * (k // 2):128 * (k % 2) + 64 * (k // 2) + 64]
                    for h in range(2):
                        ins = pe.matmul(out_bank[64 * h:64 * h + 64, 0:HF], lhs, ring[:, slot, w, k, h * HF:(h + 1) * HF],
                                        start=(k == 0), stop=(k == DC - 1), skip_group_check=True)
                ins.then_inc(s, 1)

            def by_slot(slot, body):
                with pe.If(slot < 2):
                    with pe.If(slot == 0):
                        body(0)
                    with pe.Else():
                        body(1)
                with pe.Else():
                    with pe.If(slot == 2):
                        body(2)
                    with pe.Else():
                        body(3)

            pe.wait_ge(s_place, 1)
            pe.wait_ge(s_rtab, 1)
            pe.wait_ge(s_tabd, 32)
            for u in range(3):
                lookup(u, u % 2)
            for u in range(2):
                pe.wait_ge(s_xg[u], 16)
                if u == 1:
                    pe.wait_ge(s_xgT, 1)
                xg_transpose(u)
            pe.sem_inc(s_y, 1)
            pe.wait_ge(s_w, 1)
            pe.wait_ge(s_xgT, 2)
            halves(bank[3], xgT, 0, 0, 0, s_G)
            halves(bank[4], xgT, 0, 1, 0, s_U)
            n = pe.value_load(tab_d[0:1, 3:4], min_val=MAX_TILES // 2, max_val=MAX_TILES)
            with pe.Fori(0, T_BLOCKS) as blk:
                with pe.If(blk * (2 * T_DUOS) < n):
                    with pe.Fori(0, T_DUOS) as duo:
                        for b in range(2):
                            v_ = blk * T_DUOS + duo
                            u = v_ * 2 + b
                            with pe.If(u < n):
                                hold(pe, "pe", s_h, u + 1)
                                for c in range(2):
                                    ins = pe.transpose(bank[2][:, c * 128:(c + 1) * 128], hh[:, b, c * 128:(c + 1) * 128], ident[:, :])
                                ins.then_inc(s_hTp, 1)
                            with pe.If(u + 3 < n):
                                lookup(u + 3, 1 - b)
                            with pe.If(u + 2 < n):
                                hold(pe, "pe", s_xgT, u + 2)
                                hold(pe, "pe", s_xg[b], (v_ + 2) * 16)
                                xg_transpose(b)
                            with pe.If(u + 1 < n):
                                e1 = pe.value_load(tab_d[bass.ds(u + 1, 1), 0:1], min_val=0, max_val=NX - 1)
                                hold(pe, "pe", s_w, e1 + 1)
                                def gate_up(slot):
                                    halves(bank[3 + 2 * (1 - b)], xgT, 1 - b, 0, slot, s_G)
                                    halves(bank[4 + 2 * (1 - b)], xgT, 1 - b, 1, slot, s_U)

                                by_slot(pe.snap(e1 % RING), gate_up)
                            with pe.If(u < n):
                                e0 = pe.value_load(tab_d[bass.ds(u, 1), 0:1], min_val=0, max_val=NX - 1)
                                hold(pe, "pe", s_hT, u + 1)
                                hold(pe, "pe", s_ys, u + 1)
                                by_slot(pe.snap(e0 % RING), lambda slot: halves(bank[7], hT, b, 2, slot, s_y))


_INS = ['x', 'src', 'dst', 'edge_attr_512', 'L0_gnn_path_coeffs', 'L0_gnn_path_indices', 'L0_mix_W_qkv',
        'L0_mix_random_matrix', 'L0_mix_W_out', 'L0_mix_b_out', 'L0_ffn_Wr', 'L0_ffn_sWg', 'L0_ffn_sWu',
        'L0_ffn_sWd', 'L0_ffn_Wg', 'L0_ffn_Wu', 'L0_ffn_Wd']


def kernel(**inputs):
    import numpy as _np
    import concourse.bacc as _bacc
    from concourse import mybir as _mybir
    from concourse.bass_utils import run_bass_kernel_spmd as _run

    nc = _bacc.Bacc("TRN2", target_bir_lowering=False, num_devices=1)
    arrays, args = {}, []
    for name in _INS:
        a = _np.ascontiguousarray(inputs[name])
        arrays[f"in_{name}_dram"] = a
        args.append(nc.dram_tensor(f"in_{name}_dram", a.shape, _mybir.dt.from_np(a.dtype), kind="ExternalInput").ap())
    args.append(nc.dram_tensor("out_0_dram", (625, 512), _mybir.dt.float32, kind="ExternalOutput").ap())
    gps_layer(nc, *args)
    r = _run(nc, [arrays], core_ids=[0])
    return r.results[0]["out_0_dram"]
```
